# Optimizing a Trainium2 kernel written in Bass

```python
import numpy as np
import jax
import jax.numpy as jnp

def _softmax(x, axis=-1):
    return jax.nn.softmax(x, axis=axis)

def _gelu(x):
    return jax.nn.gelu(x, approximate=True)

def _silu(x):
    return jax.nn.silu(x)

def _sigmoid(x):
    return jax.nn.sigmoid(x)

def _layernorm(x, axis=-1, eps=1e-05):
    m = jnp.mean(x, axis=axis, keepdims=True)
    v = jnp.var(x, axis=axis, keepdims=True)
    return (x - m) / jnp.sqrt(v + eps)

def _scatter_add(tgt, idx, src, axis=0):
    return tgt.at[idx].add(src)

def _segment_sum(src, seg, n):
    return jax.ops.segment_sum(src, seg, n)
kernel_name = 'mk_dlrm_tower_d1_rec_r8_ed12f3'

def setup_inputs(seed: int=0):
    np.random.seed(seed)
    _w = jnp.asarray

    def _rec_inputs():
        import jax
        import jax.numpy as jnp
        _tk = jax.random.key(seed)
        ids = jnp.stack([jax.random.randint(jax.random.fold_in(_tk, 200 + f), (512,), 0, v, jnp.int32) for f, v in enumerate([1000, 125000, 1250, 1000, 12500, 1000, 1000, 1000, 12500, 1250, 1250, 12500, 12500, 1250, 1250, 12500, 1000, 12500, 1250, 1000, 1000, 12500, 12500, 1000, 1000, 1000])], axis=1)
        tbl_0 = 0.05 * jax.random.normal(jax.random.fold_in(_tk, 500 + 0), (1000, 128), jnp.float32)
        tbl_1 = 0.05 * jax.random.normal(jax.random.fold_in(_tk, 500 + 1), (125000, 128), jnp.float32)
        tbl_2 = 0.05 * jax.random.normal(jax.random.fold_in(_tk, 500 + 2), (1250, 128), jnp.float32)
        tbl_3 = 0.05 * jax.random.normal(jax.random.fold_in(_tk, 500 + 3), (1000, 128), jnp.float32)
        tbl_4 = 0.05 * jax.random.normal(jax.random.fold_in(_tk, 500 + 4), (12500, 128), jnp.float32)
        tbl_5 = 0.05 * jax.random.normal(jax.random.fold_in(_tk, 500 + 5), (1000, 128), jnp.float32)
        tbl_6 = 0.05 * jax.random.normal(jax.random.fold_in(_tk, 500 + 6), (1000, 128), jnp.float32)
        tbl_7 = 0.05 * jax.random.normal(jax.random.fold_in(_tk, 500 + 7), (1000, 128), jnp.float32)
        tbl_8 = 0.05 * jax.random.normal(jax.random.fold_in(_tk, 500 + 8), (12500, 128), jnp.float32)
        tbl_9 = 0.05 * jax.random.normal(jax.random.fold_in(_tk, 500 + 9), (1250, 128), jnp.float32)
        tbl_10 = 0.05 * jax.random.normal(jax.random.fold_in(_tk, 500 + 10), (1250, 128), jnp.float32)
        tbl_11 = 0.05 * jax.random.normal(jax.random.fold_in(_tk, 500 + 11), (12500, 128), jnp.float32)
        tbl_12 = 0.05 * jax.random.normal(jax.random.fold_in(_tk, 500 + 12), (12500, 128), jnp.float32)
        tbl_13 = 0.05 * jax.random.normal(jax.random.fold_in(_tk, 500 + 13), (1250, 128), jnp.float32)
        tbl_14 = 0.05 * jax.random.normal(jax.random.fold_in(_tk, 500 + 14), (1250, 128), jnp.float32)
        tbl_15 = 0.05 * jax.random.normal(jax.random.fold_in(_tk, 500 + 15), (12500, 128), jnp.float32)
        tbl_16 = 0.05 * jax.random.normal(jax.random.fold_in(_tk, 500 + 16), (1000, 128), jnp.float32)
        tbl_17 = 0.05 * jax.random.normal(jax.random.fold_in(_tk, 500 + 17), (12500, 128), jnp.float32)
        tbl_18 = 0.05 * jax.random.normal(jax.random.fold_in(_tk, 500 + 18), (1250, 128), jnp.float32)
        tbl_19 = 0.05 * jax.random.normal(jax.random.fold_in(_tk, 500 + 19), (1000, 128), jnp.float32)
        tbl_20 = 0.05 * jax.random.normal(jax.random.fold_in(_tk, 500 + 20), (1000, 128), jnp.float32)
        tbl_21 = 0.05 * jax.random.normal(jax.random.fold_in(_tk, 500 + 21), (12500, 128), jnp.float32)
        tbl_22 = 0.05 * jax.random.normal(jax.random.fold_in(_tk, 500 + 22), (12500, 128), jnp.float32)
        tbl_23 = 0.05 * jax.random.normal(jax.random.fold_in(_tk, 500 + 23), (1000, 128), jnp.float32)
        tbl_24 = 0.05 * jax.random.normal(jax.random.fold_in(_tk, 500 + 24), (1000, 128), jnp.float32)
        tbl_25 = 0.05 * jax.random.normal(jax.random.fold_in(_tk, 500 + 25), (1000, 128), jnp.float32)
        _rk = jax.random.fold_in(_tk, 7)
        r_dense_features = -0.000520686 + 1.00062 * jax.random.normal(jax.random.fold_in(_rk, 101), (512, 128), jnp.float32)
        W_top1 = 0.0405887 * jax.random.normal(jax.random.fold_in(_tk, 801), (607, 512), jnp.float32)
        W_top2 = 0.0441942 * jax.random.normal(jax.random.fold_in(_tk, 802), (512, 256), jnp.float32)
        W_top3 = 0.0625 * jax.random.normal(jax.random.fold_in(_tk, 803), (256, 1), jnp.float32)
        b_top1 = jnp.zeros((512,), jnp.float32)
        b_top2 = jnp.zeros((256,), jnp.float32)
        return (r_dense_features, ids, tbl_0, tbl_1, tbl_2, tbl_3, tbl_4, tbl_5, tbl_6, tbl_7, tbl_8, tbl_9, tbl_10, tbl_11, tbl_12, tbl_13, tbl_14, tbl_15, tbl_16, tbl_17, tbl_18, tbl_19, tbl_20, tbl_21, tbl_22, tbl_23, tbl_24, tbl_25, W_top1, b_top1, W_top2, b_top2, W_top3)
    r_dense_features, ids, tbl_0, tbl_1, tbl_2, tbl_3, tbl_4, tbl_5, tbl_6, tbl_7, tbl_8, tbl_9, tbl_10, tbl_11, tbl_12, tbl_13, tbl_14, tbl_15, tbl_16, tbl_17, tbl_18, tbl_19, tbl_20, tbl_21, tbl_22, tbl_23, tbl_24, tbl_25, W_top1, b_top1, W_top2, b_top2, W_top3 = _rec_inputs()

    def _L0_rec_setup():
        import jax, jax.numpy as jnp
        import numpy as np
        B, F, D = (2048, 26, 128)
        key = jax.random.key(seed)
        k1, k2 = jax.random.split(key)
        dense_features = jax.random.normal(k1, (B, D), dtype=jnp.float32)
        sparse_values = jax.random.normal(k2, (B, F, D), dtype=jnp.float32)
        return {'dense_features': dense_features, 'sparse_values': sparse_values}
    _L0_rec_all = _L0_rec_setup()
    _L0_rec_in = {k: v for k, v in _L0_rec_all.items() if k in ()}
    del _L0_rec_all
    return {'r_dense_features': r_dense_features, 'ids': ids, 'tbl_0': tbl_0, 'tbl_1': tbl_1, 'tbl_2': tbl_2, 'tbl_3': tbl_3, 'tbl_4': tbl_4, 'tbl_5': tbl_5, 'tbl_6': tbl_6, 'tbl_7': tbl_7, 'tbl_8': tbl_8, 'tbl_9': tbl_9, 'tbl_10': tbl_10, 'tbl_11': tbl_11, 'tbl_12': tbl_12, 'tbl_13': tbl_13, 'tbl_14': tbl_14, 'tbl_15': tbl_15, 'tbl_16': tbl_16, 'tbl_17': tbl_17, 'tbl_18': tbl_18, 'tbl_19': tbl_19, 'tbl_20': tbl_20, 'tbl_21': tbl_21, 'tbl_22': tbl_22, 'tbl_23': tbl_23, 'tbl_24': tbl_24, 'tbl_25': tbl_25, 'W_top1': W_top1, 'b_top1': b_top1, 'W_top2': W_top2, 'b_top2': b_top2, 'W_top3': W_top3}

def reference(r_dense_features, ids, tbl_0, tbl_1, tbl_2, tbl_3, tbl_4, tbl_5, tbl_6, tbl_7, tbl_8, tbl_9, tbl_10, tbl_11, tbl_12, tbl_13, tbl_14, tbl_15, tbl_16, tbl_17, tbl_18, tbl_19, tbl_20, tbl_21, tbl_22, tbl_23, tbl_24, tbl_25, W_top1, b_top1, W_top2, b_top2, W_top3):
    import jax
    import jax.numpy as jnp

    def _L0_rec_ref(dense_features, sparse_values):
        import jax, jax.numpy as jnp
        import numpy as np
        B, F, D = (2048, 26, 128)
        sd = jnp.einsum('bfd,bd->bf', sparse_values, dense_features)
        ss = jnp.einsum('bfd,bgd->bfg', sparse_values, sparse_values)
        iu, ju = jnp.triu_indices(F, k=1)
        pairs = ss[:, iu, ju]
        return jnp.concatenate([dense_features, sd, pairs], axis=1)
    e = jnp.stack([tbl_0[ids[:, 0]], tbl_1[ids[:, 1]], tbl_2[ids[:, 2]], tbl_3[ids[:, 3]], tbl_4[ids[:, 4]], tbl_5[ids[:, 5]], tbl_6[ids[:, 6]], tbl_7[ids[:, 7]], tbl_8[ids[:, 8]], tbl_9[ids[:, 9]], tbl_10[ids[:, 10]], tbl_11[ids[:, 11]], tbl_12[ids[:, 12]], tbl_13[ids[:, 13]], tbl_14[ids[:, 14]], tbl_15[ids[:, 15]], tbl_16[ids[:, 16]], tbl_17[ids[:, 17]], tbl_18[ids[:, 18]], tbl_19[ids[:, 19]], tbl_20[ids[:, 20]], tbl_21[ids[:, 21]], tbl_22[ids[:, 22]], tbl_23[ids[:, 23]], tbl_24[ids[:, 24]], tbl_25[ids[:, 25]]], axis=1)
    z = _L0_rec_ref(r_dense_features, e)
    z = z.reshape(z.shape[0], -1)
    h = jnp.concatenate([z, r_dense_features], axis=1)
    h = jnp.maximum(h @ W_top1 + b_top1, 0.0)
    h = jnp.maximum(h @ W_top2 + b_top2, 0.0)
    y = h @ W_top3
    return y

_drawn_inputs = setup_inputs


def setup_inputs(seed=0):
    import zlib

    import numpy as np

    out = dict(_drawn_inputs(seed))
    spreads = {'b_top1': (0.0, 0.1), 'b_top2': (0.0, 0.1)}
    factors = {}
    for name, (base, spread) in spreads.items():
        noise = np.random.default_rng([zlib.crc32(name.encode()), seed]).standard_normal(out[name].shape)
        drawn = base * np.exp(spread * noise) if base else spread * noise
        out[name] = jnp.asarray(drawn.astype(out[name].dtype))
    for name, factor in factors.items():
        out[name] = (out[name] * factor).astype(out[name].dtype)
    return out
```

```python
import concourse.bass as bass
from concourse import mybir
from contextlib import ExitStack

F32 = mybir.dt.float32
BF16 = mybir.dt.bfloat16
FP16 = mybir.dt.float16
I32 = mybir.dt.int32
ALU = mybir.AluOpType
ACT = mybir.ActivationFunctionType

P = 128
B = 512
T = B // P
D = 128
NF = 26
NV = NF + 1
DENSE = NF
H1, H2 = 512, 256
PAIR0 = D + NF
TAIL0 = PAIR0 + NF * (NF - 1) // 2
SLOTS = 7
BIAS_Q = 2

ONEHOT = [25, 24, 23, 20, 19]
GROUPS = [[21, 22], [16, 17, 18], [12, 13, 14, 15], [8, 9, 10, 11], [4, 5, 6, 7], [0, 1, 2, 3]]
GATHERED = [f for g in GROUPS for f in g]
NG = len(GATHERED)
NO = len(ONEHOT)
ROWS = 1000
KR = 8
PR = ROWS // KR
VP = 32
RAW = 3

PHASES = [(0, SLOTS, 4)]


def pair_row(f):
    return PAIR0 + f * (NF - 1) - f * (f - 1) // 2


def dlrm_tower(nc, dense, ids, tables, w1, b1, w2, b2, w3, out):
    ctx = ExitStack()
    with ctx:
        def sb(name, shape, dt=F32):
            return ctx.enter_context(nc.sbuf_tensor(name, shape, dt))

        def pb(name, shape):
            return ctx.enter_context(nc.psum_tensor(name, shape, F32))

        def sem(name):
            return ctx.enter_context(nc.semaphore(name))

        idx = sb("idx", [P, T * NF], I32)
        idf = sb("idf", [P, T * NF])
        dense_rows = sb("dense_rows", [P, T, D])
        rows = sb("rows", [P, T, NG, D])
        raw = sb("raw", [P, RAW, KR * D])
        rest = sb("rest", [P, KR * D])
        part = sb("part", [P, 2, 3, KR * D], BF16)
        idb = sb("idb", [P, 2, B], FP16)
        onehot = sb("onehot", [P, 2, KR, B], BF16)
        row_i = sb("row_i", [P, KR], I32)
        row_of = sb("row_of", [P, KR])
        ident = sb("ident", [P, P])
        ET = sb("ET", [P, T, P * VP])
        Z = sb("Z", [P, SLOTS, T, P])
        W1s = sb("W1s", [P, SLOTS + 1, H1])
        W1d = sb("W1d", [P, 2, H1])
        W2s = sb("W2s", [P, H1 // P, H2])
        b2s = sb("b2s", [1, H2])
        ones = sb("ones", [1, P])
        W3b = sb("W3b", [P, H2])
        h1 = sb("h1", [P, 2, H1])
        h1T = sb("h1T", [P, 2, H1])
        h2w = sb("h2w", [P, H2])
        y = sb("y", [P, T])

        stage_act = pb("stage_act", [P, 512])
        stage_dve = pb("stage_dve", [P, 512])
        gram = [pb(f"gram{i}", [P, 2, 512]) for i in range(2)]
        h1_ps = pb("h1_ps", [P, 512])
        h2_ps = pb("h2_ps", [P, 512])

        ids_in = sem("ids_in")
        dense_in = sem("dense_in")
        table_in = [sem(f"table_in{i}") for i in range(NO)]
        w1_in = sem("w1_in")
        w1d_in = sem("w1d_in")
        w2_in = sem("w2_in")
        gathered = [[sem(f"gathered{t}_{g}") for g in range(len(GROUPS))] for t in range(T)]
        ident_zero = sem("ident_zero")
        ident_ready = sem("ident_ready")
        rows_ready = sem("rows_ready")
        z_const = sem("z_const")
        w1_zero = sem("w1_zero")
        dve_consts = sem("dve_consts")
        idf_ready = sem("idf_ready")
        w1_sum = sem("w1_sum")
        hi_ready = sem("hi_ready")
        rest_ready = sem("rest_ready")
        mid_ready = sem("mid_ready")
        lo_ready = sem("lo_ready")
        idb_ready = sem("idb_ready")
        onehot_ready = sem("onehot_ready")
        act_staged = sem("act_staged")
        act_taken = sem("act_taken")
        dve_staged = sem("dve_staged")
        dve_taken = sem("dve_taken")
        gram_done = sem("gram_done")
        gram_act = sem("gram_act")
        gram_dve = sem("gram_dve")
        h1_done = sem("h1_done")
        h1_relu = sem("h1_relu")
        h2_done = sem("h2_done")
        y_ready = sem("y_ready")
        y_out = sem("y_out")

        block = ctx.enter_context(nc.Block())

        def et(t):
            return ET[:, t, :].rearrange("d (b v) -> d b v", v=VP)

        def et_all(f):
            return ET[:, :, :].rearrange("d t (b v) -> d (t b) v", v=VP)[:, :, f]

        ACT_STAGED = (["dense", "look0", "T0_0", "look1", "T0_2", "look2", "T0_4"]
                      + [f"look{i}" for i in range(3, NO)]
                      + [f"T{t}_{g}" for t in range(1, T) for g in (0, 2, 4)])
        DVE_STAGED = ["ids0", "ids1", "T0_1", "ids2", "T0_3"] + [f"ids{i}" for i in range(3, NO)] + ["T0_5"]
        for t in range(T):
            DVE_STAGED += ([f"T{t + 1}_1", f"T{t + 1}_3"] if t + 1 < T else []) + [f"h1T{t}"]
            DVE_STAGED += [f"T{t + 1}_5"] if t + 1 < T else []

        GRAMS = [(t, s0, s1, m, j0) for t in range(T) for s0, s1, m in PHASES for j0 in range(0, P // 4, 2 * m)]
        PER_TILE = len(GRAMS) // T

        @block.sync
        def _(sp):
            sp.dma_start(idx[:, :], ids.rearrange("(p t) f -> p (t f)", t=T)).then_inc(ids_in, 16)
            for i, f in enumerate(ONEHOT):
                tab = tables[f].rearrange("(p k) d -> p (k d)", k=KR)
                if i >= RAW:
                    sp.wait_ge(rest_ready, i - RAW + 1)
                sp.dma_start(raw[0:112, i % RAW, :], tab[0:112, :]).then_inc(table_in[i], 16)
                sp.dma_start(raw[112:PR, i % RAW, :], tab[112:PR, :]).then_inc(table_in[i], 16)
                if i == 0:
                    sp.dma_start(dense_rows[:, :, :], dense.rearrange("(p t) d -> p t d", t=T)).then_inc(dense_in, 16)
            sp.dma_start(W1d[:, 0, :], w1[0:D, :]).then_inc(w1d_in, 16)
            sp.dma_start(W1d[:, 1, :], w1[TAIL0:TAIL0 + D, :]).then_inc(w1d_in, 16)
            sp.wait_ge(w1_zero, 1)
            for f in range(NF - 1):
                q, s = f % 4, f // 4
                sp.dma_start(W1s[32 * q + f + 1:32 * q + NF, s, :],
                             w1[pair_row(f):pair_row(f) + NF - 1 - f, :]).then_inc(w1_in, 16)
            for q in range(4):
                n = len(range(q, NF, 4))
                sp.dma_start(W1s[32 * q + DENSE:32 * q + DENSE + 1, 0:n, :],
                             w1[D + q:D + q + 4 * (n - 1) + 1:4, :].rearrange("(o s) n -> o s n", o=1)).then_inc(w1_in, 16)
            sp.dma_start(W1s[32 * BIAS_Q:32 * BIAS_Q + 1, SLOTS - 1, :],
                         b1.rearrange("(o n) -> o n", o=1)).then_inc(w1_in, 16)
            sp.dma_start(W2s[:, :, :], w2.rearrange("(c p) n -> p c n", p=P)).then_inc(w2_in, 16)
            sp.dma_start(b2s[:, :], b2.rearrange("(o n) -> o n", o=1)).then_inc(w2_in, 16)
            sp.dma_start(W3b[:, :], w3.rearrange("(o n) c -> o (n c)", o=1).broadcast_to([P, H2])).then_inc(w2_in, 16)
            sp.wait_ge(y_ready, T)
            sp.dma_start(out.rearrange("(p t) o -> p (t o)", t=T), y[:, :]).then_inc(y_out, 16)
            sp.wait_ge(y_out, 16)

        W1_LOADS = 16 * (NF - 1 + 4 + 1)
        W2_LOADS = 16 * 3

        @block.gpsimd
        def _(pool):
            pool.memset(ident[:, :], 0.0).then_inc(ident_zero, 1)
            pool.iota(row_i[:, :], pattern=[[1, KR]], base=0, channel_multiplier=KR).then_inc(rows_ready, 1)
            pool.wait_ge(ident_zero, 1)
            pool.affine_select(out=ident[:, :], in_=ident[:, :], compare_op=ALU.not_equal, fill=1.0,
                               base=0, pattern=[[-1, P]], channel_multiplier=1).then_inc(ident_ready, 1)
            pool.wait_ge(ident_ready, 1)
            pool.memset(Z[32 * BIAS_Q:32 * BIAS_Q + 32, SLOTS - 1, :, :], 1.0).then_inc(z_const, 1)
            pool.wait_ge(z_const, 1)
            pool.memset(Z[32 * BIAS_Q + 32:P, SLOTS - 1, :, :], 0.0).then_inc(z_const, 1)
            pool.wait_ge(z_const, 2)
            pool.wait_ge(ids_in, 16)
            for t in range(T):
                for g, group in enumerate(GROUPS):
                    for f in group:
                        pool.indirect_dma_start(
                            out=rows[:, t, GATHERED.index(f), :], out_offset=None, in_=tables[f],
                            in_offset=bass.IndirectOffsetOnAxis(ap=idx[:, t * NF + f:t * NF + f + 1], axis=0),
                        ).then_inc(gathered[t][g], 16)

        @block.tensor
        def _(pe):
            def stage(name):
                if name in ACT_STAGED:
                    n = ACT_STAGED.index(name)
                    if n:
                        pe.wait_ge(act_taken, n)
                    return stage_act, act_staged
                n = DVE_STAGED.index(name)
                if n:
                    pe.wait_ge(dve_taken, n)
                return stage_dve, dve_staged

            def spread_ids(i):
                bank, staged = stage(f"ids{i}")
                for t in range(T):
                    c = t * NF + ONEHOT[i]
                    last = pe.matmul(bank[:, P * t:P * (t + 1)], idf[:, c:c + 1].broadcast_to([P, P]), ident[:, :],
                                     start=True, stop=True)
                last.then_inc(staged, 1)

            def look_up(i):
                bank, staged = stage(f"look{i}")
                pe.wait_ge(onehot_ready, i + 1)
                pe.wait_ge(lo_ready, i + 1)
                for n in range(3):
                    for k in range(KR):
                        last = pe.matmul(bank[:, 0:B], part[0:PR, i % 2, n, D * k:D * (k + 1)], onehot[0:PR, i % 2, k, :],
                                         start=(n == 0 and k == 0), stop=(n == 2 and k == KR - 1))
                last.then_inc(staged, 1)

            def transposes(t, g):
                bank, staged = stage(f"T{t}_{g}")
                pe.wait_ge(gathered[t][g], 16 * len(GROUPS[g]))
                for n, f in enumerate(GROUPS[g]):
                    last = pe.transpose(bank[:, P * n:P * (n + 1)], rows[:, t, GATHERED.index(f), :], ident[:, :])
                last.then_inc(staged, 1)

            def gram_group(n):
                t, s0, s1, m, j0 = GRAMS[n]
                if n >= 2:
                    pe.wait_ge(gram_act, n - 1)
                    pe.wait_ge(gram_dve, n - 1)
                cols = min(4 * s1, NF) - 4 * s0
                for j in range(2 * m):
                    at = (j % m) * 4 * cols
                    last = pe.matmul(gram[n % 2][:, j // m, at:at + 4 * cols],
                                     ET[:, t, 4 * VP * (j0 + j):4 * VP * (j0 + j + 1)], et(t)[:, 4 * (j0 + j):4 * (j0 + j) + 4, 4 * s0:4 * s0 + cols],
                                     start=True, stop=True)
                last.then_inc(gram_done, 1)

            def layer1(t):
                if t == 0:
                    pe.wait_ge(w1_in, W1_LOADS)
                    pe.wait_ge(w1_sum, 1)
                    pe.wait_ge(z_const, 2)
                else:
                    pe.wait_ge(h1_relu, t)
                pe.matmul(h1_ps[:, :], et(t)[:, :, DENSE], W1s[:, SLOTS, :], start=True, stop=False)
                pe.wait_ge(gram_act, PER_TILE * (t + 1))
                pe.wait_ge(gram_dve, PER_TILE * (t + 1))
                for s in range(SLOTS):
                    last = pe.matmul(h1_ps[:, :], Z[:, s, t, :], W1s[:, s, :], start=False, stop=(s == SLOTS - 1))
                last.then_inc(h1_done, 1)

            def layer1_transposes(t):
                bank, staged = stage(f"h1T{t}")
                pe.wait_ge(h1_relu, t + 1)
                for c in range(H1 // P):
                    last = pe.transpose(bank[:, P * c:P * (c + 1)], h1[:, t % 2, P * c:P * (c + 1)], ident[:, :])
                last.then_inc(staged, 1)

            def layer2(t):
                if t == 0:
                    pe.wait_ge(w2_in, W2_LOADS)
                else:
                    pe.wait_ge(y_ready, t)
                pe.matmul(h2_ps[:, 0:H2], ones[:, :], b2s[:, :], start=True, stop=False)
                pe.wait_ge(dve_taken, DVE_STAGED.index(f"h1T{t}") + 1)
                for c in range(H1 // P):
                    last = pe.matmul(h2_ps[:, 0:H2], h1T[:, t % 2, P * c:P * (c + 1)], W2s[:, c, :],
                                     start=False, stop=(c == H1 // P - 1))
                last.then_inc(h2_done, 1)

            pe.wait_ge(ident_ready, 1)
            pe.wait_ge(dense_in, 16)
            for t in range(T):
                last = pe.transpose(stage_act[:, P * t:P * (t + 1)], dense_rows[:, t, :], ident[:, :])
            last.then_inc(act_staged, 1)
            pe.wait_ge(idf_ready, 1)
            pe.wait_ge(dve_consts, 1)
            spread_ids(0)
            spread_ids(1)
            look_up(0)
            transposes(0, 0)
            transposes(0, 1)
            spread_ids(2)
            look_up(1)
            transposes(0, 2)
            transposes(0, 3)
            spread_ids(3)
            look_up(2)
            transposes(0, 4)
            for i in range(3, NO):
                if i + 1 < NO:
                    spread_ids(i + 1)
                look_up(i)
            transposes(0, 5)
            for t in range(T):
                more = t + 1 < T
                if t == 0:
                    pe.wait_ge(dve_taken, DVE_STAGED.index("T0_5") + 1)
                    pe.wait_ge(act_taken, ACT_STAGED.index(f"look{NO - 1}") + 1)
                else:
                    pe.wait_ge(dve_taken, DVE_STAGED.index(f"T{t}_5") + 1)
                    pe.wait_ge(act_taken, ACT_STAGED.index(f"T{t}_4") + 1)
                for n in range(PER_TILE):
                    gram_group(PER_TILE * t + n)
                    if more and n == PER_TILE // 2 - 1:
                        transposes(t + 1, 0)
                if more:
                    transposes(t + 1, 1)
                    transposes(t + 1, 2)
                layer1(t)
                if more:
                    transposes(t + 1, 3)
                layer1_transposes(t)
                layer2(t)
                if more:
                    transposes(t + 1, 4)
                    transposes(t + 1, 5)

        def columns_of(bank, t, g):
            group = GROUPS[g]
            n = len(group)
            return (bank[:, 0:P * n].rearrange("d (f b) -> d b f", f=n),
                    et(t)[:, :, group[0]:group[0] + n])

        def z_moves(n, samples):
            t, s0, s1, m, j0 = GRAMS[n]
            cols = min(4 * s1, NF) - 4 * s0
            for q in range(4):
                ns = len(range(4 * s0 + q, 4 * s0 + cols, 4))
                for i in samples:
                    src = gram[n % 2][32 * i:32 * i + 32, :, 0:m * 4 * cols].rearrange(
                        "p b (j i c) -> p b j i c", i=4, c=cols)[:, :, :, i, q:q + 4 * (ns - 1) + 1:4]
                    dst = Z[32 * q:32 * q + 32, s0:s0 + ns, t, 4 * j0:4 * (j0 + 2 * m)].rearrange(
                        "p s (b j i) -> p b j s i", b=2, i=4)[:, :, :, :, i]
                    yield dst, src

        @block.scalar
        def _(act):
            def take(name):
                act.wait_ge(act_staged, ACT_STAGED.index(name) + 1)

            def take_look_up(i):
                take(f"look{i}")
                act.copy(et_all(ONEHOT[i]), stage_act[:, :]).then_inc(act_taken, 1)

            def take_transposes(t, g):
                take(f"T{t}_{g}")
                src, dst = columns_of(stage_act, t, g)
                act.copy(dst, src).then_inc(act_taken, 1)

            def split(i):
                act.wait_ge(table_in[i], 32)
                if i >= 2:
                    act.wait_ge(act_staged, ACT_STAGED.index(f"look{i - 2}") + 1)
                act.copy(part[0:PR, i % 2, 0, :], raw[0:PR, i % RAW, :]).then_inc(hi_ready, 1)
                act.wait_ge(rest_ready, i + 1)
                act.copy(part[0:PR, i % 2, 1, :], rest[0:PR, :]).then_inc(mid_ready, 1)

            def move_gram(n):
                act.wait_ge(gram_done, n + 1)
                for dst, src in z_moves(n, (2, 3)):
                    last = act.copy(dst, src)
                last.then_inc(gram_act, 1)

            take("dense")
            act.copy(et_all(DENSE), stage_act[:, :]).then_inc(act_taken, 1)
            split(0)
            split(1)
            take_look_up(0)
            take_transposes(0, 0)
            split(2)
            take_look_up(1)
            take_transposes(0, 2)
            split(3)
            take_look_up(2)
            take_transposes(0, 4)
            for i in range(3, NO):
                if i + 1 < NO:
                    split(i + 1)
                take_look_up(i)
            for t in range(T):
                more = t + 1 < T
                for n in range(PER_TILE):
                    move_gram(PER_TILE * t + n)
                    if more and n == PER_TILE // 2 - 1:
                        take_transposes(t + 1, 0)
                if more:
                    take_transposes(t + 1, 2)
                act.wait_ge(h1_done, t + 1)
                act.activation(h1[:, t % 2, :], h1_ps[:, :], ACT.Relu).then_inc(h1_relu, 1)
                if more:
                    take_transposes(t + 1, 4)

        @block.vector
        def _(dve):
            def take(name):
                dve.wait_ge(dve_staged, DVE_STAGED.index(name) + 1)

            def take_transposes(t, g):
                take(f"T{t}_{g}")
                src, dst = columns_of(stage_dve, t, g)
                dve.tensor_copy(dst, src).then_inc(dve_taken, 1)

            def make_onehot(i):
                take(f"ids{i}")
                dve.tensor_copy(idb[:, i % 2, :], stage_dve[:, 0:B]).then_inc(dve_taken, 1)
                dve.wait_ge(dve_taken, DVE_STAGED.index(f"ids{i}") + 1)
                if i >= 2:
                    dve.wait_ge(act_staged, ACT_STAGED.index(f"look{i - 2}") + 1)
                for k in range(KR):
                    last = dve.tensor_scalar(onehot[0:PR, i % 2, k, :], idb[0:PR, i % 2, :], row_of[0:PR, k:k + 1], None,
                                             ALU.is_equal)
                last.then_inc(onehot_ready, 1)

            def split(i):
                dve.wait_ge(table_in[i], 32)
                dve.wait_ge(hi_ready, i + 1)
                dve.tensor_tensor(rest[0:PR, :], raw[0:PR, i % RAW, :], part[0:PR, i % 2, 0, :],
                                  ALU.subtract).then_inc(rest_ready, 1)
                dve.wait_ge(mid_ready, i + 1)
                dve.tensor_tensor(part[0:PR, i % 2, 2, :], rest[0:PR, :], part[0:PR, i % 2, 1, :],
                                  ALU.subtract).then_inc(lo_ready, 1)

            def move_gram(n):
                dve.wait_ge(gram_done, n + 1)
                for dst, src in z_moves(n, (0, 1)):
                    last = dve.tensor_copy(dst, src)
                last.then_inc(gram_dve, 1)

            dve.memset(ET[:, :, :].rearrange("d t (b v) -> d (t b) v", v=VP)[:, :, NV:VP], 0.0)
            dve.memset(ones[:, :], 1.0).then_inc(dve_consts, 1)
            dve.wait_ge(ids_in, 16)
            dve.tensor_copy(idf[:, :], idx[:, :]).then_inc(idf_ready, 1)
            dve.wait_ge(rows_ready, 1)
            dve.tensor_copy(row_of[:, :], row_i[:, :]).then_inc(rows_ready, 1)
            dve.wait_ge(rows_ready, 2)
            make_onehot(0)
            split(0)
            dve.memset(W1s[:, 0:SLOTS, :], 0.0).then_inc(w1_zero, 1)
            make_onehot(1)
            split(1)
            take_transposes(0, 1)
            make_onehot(2)
            split(2)
            take_transposes(0, 3)
            for i in range(3, NO):
                make_onehot(i)
                split(i)
            take_transposes(0, 5)
            dve.wait_ge(w1d_in, 32)
            dve.tensor_tensor(W1s[:, SLOTS, :], W1d[:, 0, :], W1d[:, 1, :], ALU.add).then_inc(w1_sum, 1)
            for t in range(T):
                more = t + 1 < T
                for n in range(PER_TILE):
                    move_gram(PER_TILE * t + n)
                if more:
                    take_transposes(t + 1, 1)
                    take_transposes(t + 1, 3)
                take(f"h1T{t}")
                dve.tensor_copy(h1T[:, t % 2, :], stage_dve[:, :]).then_inc(dve_taken, 1)
                dve.wait_ge(h2_done, t + 1)
                dve.wait_ge(w2_in, W2_LOADS)
                dve.scalar_tensor_tensor(out=h2w[:, :], in0=h2_ps[:, 0:H2], scalar=0.0, in1=W3b[:, :],
                                         op0=ALU.max, op1=ALU.mult, accum_out=y[:, t:t + 1]).then_inc(y_ready, 1)
                if more:
                    take_transposes(t + 1, 5)


_INPUTS = (['r_dense_features', 'ids'] + [f'tbl_{f}' for f in range(NF)]
           + ['W_top1', 'b_top1', 'W_top2', 'b_top2', 'W_top3'])


def kernel(**inputs):
    import numpy as np
    import concourse.bacc as bacc
    from concourse.bass_utils import run_bass_kernel_spmd

    nc = bacc.Bacc("TRN2", target_bir_lowering=False, num_devices=1)
    arrays, aps = {}, []
    for name in _INPUTS:
        a = np.ascontiguousarray(inputs[name])
        arrays[name] = a
        aps.append(nc.dram_tensor(name, a.shape, mybir.dt.from_np(a.dtype), kind="ExternalInput").ap())
    out = nc.dram_tensor("out", (B, 1), F32, kind="ExternalOutput").ap()
    dlrm_tower(nc, aps[0], aps[1], aps[2:2 + NF], *aps[2 + NF:], out)
    r = run_bass_kernel_spmd(nc, [arrays], core_ids=[0])
    return r.results[0]["out"]
```

```python
import concourse.bass as bass
from concourse import mybir
from contextlib import ExitStack

F32 = mybir.dt.float32
BF16 = mybir.dt.bfloat16
FP16 = mybir.dt.float16
FP32R = mybir.dt.float32r
I32 = mybir.dt.int32
ALU = mybir.AluOpType
ACT = mybir.ActivationFunctionType

P = 128
B = 512
T = B // P
D = 128
NF = 26
NV = NF + 1
DENSE = NF
H1, H2 = 512, 256
PAIR0 = D + NF
TAIL0 = PAIR0 + NF * (NF - 1) // 2
SLOTS = 7
BIAS_Q = 2

ONEHOT = [25, 24, 23, 20, 19, 16]
GROUPS = [[21, 22], [17, 18], [12, 13, 14, 15], [8, 9, 10, 11], [4, 5, 6, 7], [0, 1, 2, 3]]
GATHERED = [f for g in GROUPS for f in g]
NG = len(GATHERED)
NO = len(ONEHOT)
ROWS = 1000
KR = 8
PR = ROWS // KR
VP = 32
RAW = 3

GP = 4
GG = P // 4 // (2 * GP)


def pair_row(f):
    return PAIR0 + f * (NF - 1) - f * (f - 1) // 2


def dlrm_tower(nc, dense, ids, tables, w1, b1, w2, b2, w3, out):
    ctx = ExitStack()
    with ctx:
        def sb(name, shape, dt=F32):
            return ctx.enter_context(nc.sbuf_tensor(name, shape, dt))

        def pb(name, shape):
            return ctx.enter_context(nc.psum_tensor(name, shape, F32))

        def sem(name):
            return ctx.enter_context(nc.semaphore(name))

        idx = sb("idx", [P, T * NF], I32)
        idh = sb("idh", [P, T * NF], FP16)
        dense_rows = sb("dense_rows", [P, T, D])
        rows = sb("rows", [P, 2, NG, D])
        raw = sb("raw", [P, RAW, KR * D])
        part = sb("part", [P, 2, 2, KR * D], FP32R)
        idb = sb("idb", [P, 2, B], FP16)
        onehot = sb("onehot", [P, 2, KR, B], FP32R)
        row_i = sb("row_i", [P, KR], I32)
        row_of = sb("row_of", [P, KR])
        ident = sb("ident", [P, P])
        ident_h = sb("ident_h", [P, P], FP16)
        ET = sb("ET", [P, T, P * VP])
        Z = sb("Z", [P, SLOTS, T, P])
        W1s = sb("W1s", [P, SLOTS + 1, H1])
        W1d = sb("W1d", [P, 2, H1])
        W2s = sb("W2s", [P, H1 // P, H2])
        b2s = sb("b2s", [3, H2])
        b2m = sb("b2m", [3, 2, H2])
        b2p = sb("b2p", [3, 3, H2], BF16)
        b2k = sb("b2k", [3, H2], BF16)
        ones = sb("ones", [3, P], BF16)
        zero = sb("zero", [P, 1])
        W3b = sb("W3b", [P, H2])
        h1 = sb("h1", [P, 2, H1])
        h1T = sb("h1T", [P, 2, H1])
        h2w = sb("h2w", [P, H2])
        y = sb("y", [P, T])

        stage_act = pb("stage_act", [P, 512])
        stage_dve = pb("stage_dve", [P, 512])
        gram = [pb(f"gram{i}", [P, 2, 512]) for i in range(2)]
        h1_ps = pb("h1_ps", [P, 512])
        h2_ps = pb("h2_ps", [P, 512])

        ids_in = sem("ids_in")
        dense_in = sem("dense_in")
        table_in = [sem(f"table_in{i}") for i in range(NO)]
        w1_in = sem("w1_in")
        w1d_in = sem("w1d_in")
        w2_in = sem("w2_in")
        gathered = [[sem(f"gathered{t}_{g}") for g in range(len(GROUPS))] for t in range(T)]
        ident_zero = sem("ident_zero")
        ident_ready = sem("ident_ready")
        rows_ready = sem("rows_ready")
        z_const = sem("z_const")
        w1_zero = sem("w1_zero")
        dve_consts = sem("dve_consts")
        idh_ready = sem("idh_ready")
        b2_in = sem("b2_in")
        b2_step = sem("b2_step")
        w1_sum = sem("w1_sum")
        hi_ready = sem("hi_ready")
        lo_ready = sem("lo_ready")
        idb_ready = sem("idb_ready")
        onehot_ready = sem("onehot_ready")
        act_staged = sem("act_staged")
        act_taken = sem("act_taken")
        dve_staged = sem("dve_staged")
        dve_taken = sem("dve_taken")
        look_done = sem("look_done")
        look_taken = sem("look_taken")
        gram_done = sem("gram_done")
        gram_act = sem("gram_act")
        gram_dve = sem("gram_dve")
        h1_done = sem("h1_done")
        h1_relu = sem("h1_relu")
        h2_done = sem("h2_done")
        y_ready = sem("y_ready")
        y_out = sem("y_out")

        block = ctx.enter_context(nc.Block())

        def et(t):
            return ET[:, t, :].rearrange("d (b v) -> d b v", v=VP)

        def et_all(f):
            return ET[:, :, :].rearrange("d t (b v) -> d (t b) v", v=VP)[:, :, f]

        ACT_STAGED = ["dense"] + [f"T0_{g}" for g in range(len(GROUPS))]
        DVE_STAGED = [f"ids{i}" for i in range(NO)]
        for t in range(T):
            if t + 1 < T:
                ACT_STAGED += [f"T{t + 1}_{g}" for g in (0, 2, 4, 5)]
                DVE_STAGED += [f"T{t + 1}_1", f"T{t + 1}_3"]
            DVE_STAGED += [f"h1T{t}"]

        def look_bank(i):
            return h2_ps if i % 2 else h1_ps

        def taken(name):
            if name in ACT_STAGED:
                return act_taken, ACT_STAGED.index(name) + 1
            return dve_taken, DVE_STAGED.index(name) + 1

        @block.sync
        def _(sp):
            sp.dma_start(idx[:, :], ids.rearrange("(p t) f -> p (t f)", t=T)).then_inc(ids_in, 16)
            for i, f in enumerate(ONEHOT):
                tab = tables[f].rearrange("(p k) d -> p (k d)", k=KR)
                if i >= RAW:
                    sp.wait_ge(lo_ready, i - RAW + 1)
                sp.dma_start(raw[0:112, i % RAW, :], tab[0:112, :]).then_inc(table_in[i], 16)
                sp.dma_start(raw[112:PR, i % RAW, :], tab[112:PR, :]).then_inc(table_in[i], 16)
                if i == 1:
                    sp.dma_start(dense_rows[:, :, :], dense.rearrange("(p t) d -> p t d", t=T)).then_inc(dense_in, 16)
            for n in range(3):
                sp.dma_start(b2s[n:n + 1, :], b2.rearrange("(o n) -> o n", o=1)).then_inc(b2_in, 16)
            sp.dma_start(W1d[:, 0, :], w1[0:D, :]).then_inc(w1d_in, 16)
            sp.dma_start(W1d[:, 1, :], w1[TAIL0:TAIL0 + D, :]).then_inc(w1d_in, 16)
            sp.wait_ge(w1_zero, 1)
            for f in range(NF - 1):
                q, s = f % 4, f // 4
                sp.dma_start(W1s[32 * q + f + 1:32 * q + NF, s, :],
                             w1[pair_row(f):pair_row(f) + NF - 1 - f, :]).then_inc(w1_in, 16)
            for q in range(4):
                n = len(range(q, NF, 4))
                sp.dma_start(W1s[32 * q + DENSE:32 * q + DENSE + 1, 0:n, :],
                             w1[D + q:D + q + 4 * (n - 1) + 1:4, :].rearrange("(o s) n -> o s n", o=1)).then_inc(w1_in, 16)
            sp.dma_start(W1s[32 * BIAS_Q:32 * BIAS_Q + 1, SLOTS - 1, :],
                         b1.rearrange("(o n) -> o n", o=1)).then_inc(w1_in, 16)
            sp.dma_start(W2s[:, :, :], w2.rearrange("(c p) n -> p c n", p=P)).then_inc(w2_in, 16)
            sp.dma_start(W3b[:, :], w3.rearrange("(o n) c -> o (n c)", o=1).broadcast_to([P, H2])).then_inc(w2_in, 16)
            sp.wait_ge(y_ready, T)
            sp.dma_start(out.rearrange("(p t) o -> p (t o)", t=T), y[:, :]).then_inc(y_out, 16)
            sp.wait_ge(y_out, 16)

        W1_LOADS = 16 * (NF - 1 + 4 + 1)
        W2_LOADS = 16 * 2

        @block.gpsimd
        def _(pool):
            pool.memset(ident[:, :], 0.0).then_inc(ident_zero, 1)
            pool.iota(row_i[:, :], pattern=[[1, KR]], base=0, channel_multiplier=KR).then_inc(rows_ready, 1)
            pool.wait_ge(ident_zero, 1)
            pool.affine_select(out=ident[:, :], in_=ident[:, :], compare_op=ALU.not_equal, fill=1.0,
                               base=0, pattern=[[-1, P]], channel_multiplier=1).then_inc(ident_ready, 1)
            pool.wait_ge(ident_ready, 1)
            pool.memset(Z[32 * BIAS_Q:32 * BIAS_Q + 32, SLOTS - 1, :, :], 1.0).then_inc(z_const, 1)
            pool.wait_ge(z_const, 1)
            pool.memset(Z[32 * BIAS_Q + 32:P, SLOTS - 1, :, :], 0.0).then_inc(z_const, 1)
            pool.wait_ge(z_const, 2)
            pool.wait_ge(ids_in, 16)
            for t in range(T):
                for g, group in enumerate(GROUPS):
                    if t >= 2:
                        pool.wait_ge(*taken(f"T{t - 2}_{g}"))
                    for f in group:
                        pool.indirect_dma_start(
                            out=rows[:, t % 2, GATHERED.index(f), :], out_offset=None, in_=tables[f],
                            in_offset=bass.IndirectOffsetOnAxis(ap=idx[:, t * NF + f:t * NF + f + 1], axis=0),
                        ).then_inc(gathered[t][g], 16)

        @block.tensor
        def _(pe):
            def stage(name):
                if name in ACT_STAGED:
                    n = ACT_STAGED.index(name)
                    if n:
                        pe.wait_ge(act_taken, n)
                    return stage_act, act_staged
                n = DVE_STAGED.index(name)
                if n:
                    pe.wait_ge(dve_taken, n)
                return stage_dve, dve_staged

            def spread_ids(i):
                bank, staged = stage(f"ids{i}")
                for t in range(T):
                    c = t * NF + ONEHOT[i]
                    last = pe.matmul(bank[:, P * t:P * (t + 1)], idh[:, c:c + 1].broadcast_to([P, P]), ident_h[:, :],
                                     start=True, stop=True)
                last.then_inc(staged, 1)

            def look_up(i):
                if i >= 2:
                    pe.wait_ge(look_taken, i - 1)
                pe.wait_ge(hi_ready, i + 1)
                for n in range(2):
                    for k in range(KR):
                        if n == 0:
                            pe.wait_ge(onehot_ready, KR * i + k + 1)
                        elif k == 0:
                            pe.wait_ge(lo_ready, i + 1)
                        last = pe.matmul(look_bank(i)[:, 0:B], part[0:PR, i % 2, n, D * k:D * (k + 1)],
                                         onehot[0:PR, i % 2, k, :],
                                         start=(n == 0 and k == 0), stop=(n == 1 and k == KR - 1))
                last.then_inc(look_done, 1)

            def transposes(t, g):
                bank, staged = stage(f"T{t}_{g}")
                pe.wait_ge(gathered[t][g], 16 * len(GROUPS[g]))
                for n, f in enumerate(GROUPS[g]):
                    last = pe.transpose(bank[:, P * n:P * (n + 1)], rows[:, t % 2, GATHERED.index(f), :], ident[:, :])
                last.then_inc(staged, 1)

            def gram_group(n):
                t, j0 = n // GG, n % GG * 2 * GP
                if n >= 2:
                    pe.wait_ge(gram_act, n - 1)
                    pe.wait_ge(gram_dve, n - 1)
                for j in range(2 * GP):
                    at = (j % GP) * 4 * NF
                    last = pe.matmul(gram[n % 2][:, j // GP, at:at + 4 * NF],
                                     ET[:, t, 4 * VP * (j0 + j):4 * VP * (j0 + j + 1)],
                                     et(t)[:, 4 * (j0 + j):4 * (j0 + j) + 4, 0:NF],
                                     start=True, stop=True)
                last.then_inc(gram_done, 1)

            def layer1(t):
                if t == 0:
                    pe.wait_ge(w1_in, W1_LOADS)
                    pe.wait_ge(w1_sum, 1)
                    pe.wait_ge(z_const, 2)
                    pe.wait_ge(look_taken, NO)
                else:
                    pe.wait_ge(h1_relu, t)
                pe.matmul(h1_ps[:, :], et(t)[:, :, DENSE], W1s[:, SLOTS, :], start=True, stop=False)
                pe.wait_ge(gram_act, GG * (t + 1))
                pe.wait_ge(gram_dve, GG * (t + 1))
                for s in range(SLOTS):
                    last = pe.matmul(h1_ps[:, :], Z[:, s, t, :], W1s[:, s, :], start=False, stop=(s == SLOTS - 1))
                last.then_inc(h1_done, 1)

            def layer1_transposes(t):
                bank, staged = stage(f"h1T{t}")
                pe.wait_ge(h1_relu, t + 1)
                for c in range(H1 // P):
                    last = pe.transpose(bank[:, P * c:P * (c + 1)], h1[:, t % 2, P * c:P * (c + 1)], ident[:, :])
                last.then_inc(staged, 1)

            def layer2(t):
                if t == 0:
                    pe.wait_ge(w2_in, W2_LOADS)
                    pe.wait_ge(b2_step, 7)
                else:
                    pe.wait_ge(y_ready, t)
                pe.matmul(h2_ps[:, 0:H2], ones[:, :], b2k[:, :], start=True, stop=False)
                pe.wait_ge(dve_taken, DVE_STAGED.index(f"h1T{t}") + 1)
                for c in range(H1 // P):
                    last = pe.matmul(h2_ps[:, 0:H2], h1T[:, t % 2, P * c:P * (c + 1)], W2s[:, c, :],
                                     start=False, stop=(c == H1 // P - 1))
                last.then_inc(h2_done, 1)

            pe.wait_ge(idh_ready, 2)
            spread_ids(0)
            pe.wait_ge(ident_ready, 1)
            pe.wait_ge(dense_in, 16)
            for t in range(T):
                last = pe.transpose(stage_act[:, P * t:P * (t + 1)], dense_rows[:, t, :], ident[:, :])
            last.then_inc(act_staged, 1)
            for i in range(NO):
                if i + 1 < NO:
                    spread_ids(i + 1)
                look_up(i)
                transposes(0, i)
            for t in range(T):
                more = t + 1 < T
                if t == 0:
                    pe.wait_ge(look_taken, NO)
                else:
                    pe.wait_ge(*taken(f"T{t}_3"))
                pe.wait_ge(*taken(f"T{t}_5"))
                for n in range(GG):
                    gram_group(GG * t + n)
                    if more and n == 1:
                        transposes(t + 1, 0)
                        transposes(t + 1, 1)
                if more:
                    transposes(t + 1, 2)
                layer1(t)
                if more:
                    transposes(t + 1, 3)
                    transposes(t + 1, 4)
                layer1_transposes(t)
                if more:
                    transposes(t + 1, 5)
                layer2(t)

        def columns_of(bank, t, g):
            group = GROUPS[g]
            n = len(group)
            return (bank[:, 0:P * n].rearrange("d (f b) -> d b f", f=n),
                    et(t)[:, :, group[0]:group[0] + n])

        def z_moves(n, samples):
            t, j0 = n // GG, n % GG * 2 * GP
            for q in range(4):
                ns = len(range(q, NF, 4))
                for i in samples:
                    src = gram[n % 2][32 * i:32 * i + 32, :, 0:GP * 4 * NF].rearrange(
                        "p b (j i c) -> p b j i c", i=4, c=NF)[:, :, :, i, q:q + 4 * (ns - 1) + 1:4]
                    dst = Z[32 * q:32 * q + 32, 0:ns, t, 4 * j0:4 * (j0 + 2 * GP)].rearrange(
                        "p s (b j i) -> p b j s i", b=2, i=4)[:, :, :, :, i]
                    yield dst, src

        @block.scalar
        def _(act):
            def take(name):
                act.wait_ge(act_staged, ACT_STAGED.index(name) + 1)

            def take_look_up(i):
                act.wait_ge(look_done, i + 1)
                act.copy(et_all(ONEHOT[i]), look_bank(i)[:, :]).then_inc(look_taken, 1)

            def take_transposes(t, g):
                take(f"T{t}_{g}")
                src, dst = columns_of(stage_act, t, g)
                act.copy(dst, src).then_inc(act_taken, 1)

            def relu(t):
                act.wait_ge(h1_done, t + 1)
                act.activation(h1[:, t % 2, :], h1_ps[:, :], ACT.Relu).then_inc(h1_relu, 1)

            def upper_part(i):
                act.wait_ge(table_in[i], 32)
                if i >= 2:
                    act.wait_ge(look_done, i - 1)
                act.copy(part[0:PR, i % 2, 0, :], raw[0:PR, i % RAW, :]).then_inc(hi_ready, 1)

            def move_gram(n):
                act.wait_ge(gram_done, n + 1)
                for dst, src in z_moves(n, (2, 3)):
                    last = act.copy(dst, src)
                last.then_inc(gram_act, 1)

            take("dense")
            act.copy(et_all(DENSE), stage_act[:, :]).then_inc(act_taken, 1)
            upper_part(0)
            act.wait_ge(dve_consts, 1)
            act.copy(W1s[:, 0:SLOTS, :].rearrange("p s n -> p (s n)"), zero[:, :].broadcast_to([P, SLOTS * H1])).then_inc(w1_zero, 1)
            upper_part(1)
            for i in range(NO):
                take_look_up(i)
                if i + 2 < NO:
                    upper_part(i + 2)
                take_transposes(0, i)
            for t in range(T):
                more = t + 1 < T
                for n in range(GG):
                    move_gram(GG * t + n)
                    if more and n == 1:
                        take_transposes(t + 1, 0)
                if more:
                    take_transposes(t + 1, 2)
                relu(t)
                if more:
                    take_transposes(t + 1, 4)
                    take_transposes(t + 1, 5)

        @block.vector
        def _(dve):
            def take(name):
                dve.wait_ge(dve_staged, DVE_STAGED.index(name) + 1)

            def take_transposes(t, g):
                take(f"T{t}_{g}")
                src, dst = columns_of(stage_dve, t, g)
                dve.tensor_copy(dst, src).then_inc(dve_taken, 1)

            def take_h1(t):
                take(f"h1T{t}")
                dve.tensor_copy(h1T[:, t % 2, :], stage_dve[:, :]).then_inc(dve_taken, 1)

            def last_layer(t):
                dve.wait_ge(h2_done, t + 1)
                dve.wait_ge(w2_in, W2_LOADS)
                dve.scalar_tensor_tensor(out=h2w[:, :], in0=h2_ps[:, 0:H2], scalar=0.0, in1=W3b[:, :],
                                         op0=ALU.max, op1=ALU.mult, accum_out=y[:, t:t + 1]).then_inc(y_ready, 1)

            def make_onehot(i):
                take(f"ids{i}")
                dve.tensor_copy(idb[:, i % 2, :], stage_dve[:, 0:B]).then_inc(dve_taken, 1)
                dve.wait_ge(dve_taken, DVE_STAGED.index(f"ids{i}") + 1)
                if i >= 2:
                    dve.wait_ge(look_done, i - 1)
                for k in range(KR):
                    dve.tensor_scalar(onehot[0:PR, i % 2, k, :], idb[0:PR, i % 2, :], row_of[0:PR, k:k + 1], None,
                                             ALU.is_equal).then_inc(onehot_ready, 1)

            def lower_part(i):
                dve.wait_ge(table_in[i], 32)
                dve.wait_ge(hi_ready, i + 1)
                dve.tensor_tensor(part[0:PR, i % 2, 1, :], raw[0:PR, i % RAW, :], part[0:PR, i % 2, 0, :].bitcast(F32),
                                  ALU.subtract).then_inc(lo_ready, 1)

            def move_gram(n):
                dve.wait_ge(gram_done, n + 1)
                for dst, src in z_moves(n, (0, 1)):
                    last = dve.tensor_copy(dst, src)
                last.then_inc(gram_dve, 1)

            dve.memset(ET[:, :, :].rearrange("d t (b v) -> d (t b) v", v=VP)[:, :, NV:VP], 0.0)
            dve.memset(zero[:, :], 0.0).then_inc(dve_consts, 1)
            dve.wait_ge(ident_ready, 1)
            dve.tensor_copy(ident_h[:, :], ident[:, :]).then_inc(idh_ready, 1)
            dve.wait_ge(ids_in, 16)
            dve.tensor_copy(idh[:, :], idx[:, :]).then_inc(idh_ready, 1)
            dve.wait_ge(rows_ready, 1)
            dve.tensor_copy(row_of[:, :], row_i[:, :]).then_inc(rows_ready, 1)
            dve.wait_ge(rows_ready, 2)
            for i in range(NO):
                make_onehot(i)
                lower_part(i)
            dve.memset(ones[:, :], 1.0).then_inc(dve_consts, 1)
            dve.wait_ge(b2_in, 48)
            dve.tensor_copy(b2p[:, 0, :], b2s[:, :]).then_inc(b2_step, 1)
            dve.wait_ge(b2_step, 1)
            dve.tensor_tensor(b2m[:, 0, :], b2s[:, :], b2p[:, 0, :], ALU.subtract).then_inc(b2_step, 1)
            dve.wait_ge(b2_step, 2)
            dve.tensor_copy(b2p[:, 1, :], b2m[:, 0, :]).then_inc(b2_step, 1)
            dve.wait_ge(b2_step, 3)
            dve.tensor_tensor(b2m[:, 1, :], b2m[:, 0, :], b2p[:, 1, :], ALU.subtract).then_inc(b2_step, 1)
            dve.wait_ge(b2_step, 4)
            dve.tensor_copy(b2k[0:3, :], b2m[:, 1, :]).then_inc(b2_step, 1)
            dve.wait_ge(b2_step, 5)
            dve.tensor_copy(b2k[0:2, :], b2p[0:2, 1, :]).then_inc(b2_step, 1)
            dve.wait_ge(b2_step, 6)
            dve.tensor_copy(b2k[0:1, :], b2p[0:1, 0, :]).then_inc(b2_step, 1)
            dve.wait_ge(w1d_in, 32)
            dve.tensor_tensor(W1s[:, SLOTS, :], W1d[:, 0, :], W1d[:, 1, :], ALU.add).then_inc(w1_sum, 1)
            for t in range(T):
                more = t + 1 < T
                for n in range(GG):
                    move_gram(GG * t + n)
                    if more and n == 1:
                        take_transposes(t + 1, 1)
                if more:
                    take_transposes(t + 1, 3)
                take_h1(t)
                last_layer(t)


_INPUTS = (['r_dense_features', 'ids'] + [f'tbl_{f}' for f in range(NF)]
           + ['W_top1', 'b_top1', 'W_top2', 'b_top2', 'W_top3'])


def kernel(**inputs):
    import numpy as np
    import concourse.bacc as bacc
    from concourse.bass_utils import run_bass_kernel_spmd

    nc = bacc.Bacc("TRN2", target_bir_lowering=False, num_devices=1)
    arrays, aps = {}, []
    for name in _INPUTS:
        a = np.ascontiguousarray(inputs[name])
        arrays[name] = a
        aps.append(nc.dram_tensor(name, a.shape, mybir.dt.from_np(a.dtype), kind="ExternalInput").ap())
    out = nc.dram_tensor("out", (B, 1), F32, kind="ExternalOutput").ap()
    dlrm_tower(nc, aps[0], aps[1], aps[2:2 + NF], *aps[2 + NF:], out)
    r = run_bass_kernel_spmd(nc, [arrays], core_ids=[0])
    return r.results[0]["out"]
```

```python
import concourse.bass as bass
from concourse import mybir
from contextlib import ExitStack

F32 = mybir.dt.float32
BF16 = mybir.dt.bfloat16
FP16 = mybir.dt.float16
FP32R = mybir.dt.float32r
I32 = mybir.dt.int32
ALU = mybir.AluOpType
ACT = mybir.ActivationFunctionType

P = 128
B = 512
T = B // P
D = 128
NF = 26
NV = NF + 1
DENSE = NF
H1, H2 = 512, 256
PAIR0 = D + NF
TAIL0 = PAIR0 + NF * (NF - 1) // 2
SLOTS = 7
FOLD = 3
FOLDED = 4 * FOLD
WSLOTS = FOLD + 1
HC = H1 // P

ONEHOT = [25, 24, 23, 20, 19, 16, 0, 7]
HALF = 7
HALF_FROM = 2
GROUPS = [[1, 2, 3, 4], [5, 6, 7], [8, 9, 10, 11], [12, 13, 14, 15], [17, 18], [21, 22]]
GATHERED = [f for g in GROUPS for f in g]
NG = len(GATHERED)
NO = len(ONEHOT)
ROWS = 1000
KR = 8
PR = ROWS // KR
VP = 32
RAW = 3

GP = 4
GG = P // 4 // (2 * GP)


def group_of(t, g):
    return [f for f in GROUPS[g] if t < HALF_FROM or f != HALF]


def looked_up(i):
    return slice(P * HALF_FROM if ONEHOT[i] == HALF else 0, B)


def pair_row(f):
    return PAIR0 + f * (NF - 1) - f * (f - 1) // 2


def dlrm_tower(nc, dense, ids, tables, w1, b1, w2, b2, w3, out):
    ctx = ExitStack()
    with ctx:
        def sb(name, shape, dt=F32):
            return ctx.enter_context(nc.sbuf_tensor(name, shape, dt))

        def pb(name, shape):
            return ctx.enter_context(nc.psum_tensor(name, shape, F32))

        def sem(name):
            return ctx.enter_context(nc.semaphore(name))

        idx = sb("idx", [P, T * NF], I32)
        idh = sb("idh", [P, T * NF], FP16)
        dense_rows = sb("dense_rows", [P, T, D])
        rows = sb("rows", [P, 2, NG, D])
        raw = sb("raw", [P, RAW, KR * D])
        part = sb("part", [P, 2, 2, KR * D], FP32R)
        idb = sb("idb", [P, NO, B], FP16)
        onehot = sb("onehot", [P, 2, KR, B], FP32R)
        row_i = sb("row_i", [P, 1], I32)
        first_row = sb("first_row", [P, 1])
        ident = sb("ident", [P, P])
        ident_h = sb("ident_h", [P, P], FP16)
        ET = sb("ET", [P, T, P * VP])
        Z = sb("Z", [P, 2, SLOTS, P])
        W1s = sb("W1s", [P, WSLOTS, H1])
        behind_i = sb("behind_i", [P, FOLD], I32)
        behind = sb("behind", [P, FOLD])
        fold_f = sb("fold_f", [P, FOLD])
        fold_mask = sb("fold_mask", [P, FOLD, 8 * GP], I32)
        W1d = sb("W1d", [P, 2, H1])
        W1e = sb("W1e", [P, H1])
        b1c = sb("b1c", [P, HC])
        W2s = sb("W2s", [P, H1 // P, H2])
        b2p = sb("b2p", [3, 3, H2], BF16)
        b2k = sb("b2k", [3, H2], BF16)
        ones = sb("ones", [3, P], BF16)
        zero = sb("zero", [P, 1])
        warm = sb("warm", [P, 1])
        W3b = sb("W3b", [P, H2])
        h1T = sb("h1T", [P, 2, HC, P])
        b2s = sb("b2s", [3, H2])
        b2m = sb("b2m", [3, 2, H2])
        h2w = sb("h2w", [P, H2])
        y = sb("y", [P, T])

        stage = pb("stage", [P, 512])
        second = pb("second", [P, 512])
        gram = [pb(f"gram{i}", [P, 2, 512]) for i in range(2)]
        hidden = [pb(f"hidden{i}", [P, 512]) for i in range(2)]
        H1_BANKS = [gram[0][:, 0, :], gram[0][:, 1, :], hidden[0], hidden[1]]

        ids_in = sem("ids_in")
        dense_in = sem("dense_in")
        table_in = [sem(f"table_in{i}") for i in range(NO)]
        w1_in = sem("w1_in")
        w1d_in = sem("w1d_in")
        w2_in = sem("w2_in")
        gathered = [[sem(f"gathered{t}_{g}") for g in range(len(GROUPS))] for t in range(T)]
        ident_zero = sem("ident_zero")
        ident_ready = sem("ident_ready")
        rows_ready = sem("rows_ready")
        behind_ready = sem("behind_ready")
        mask_step = sem("mask_step")
        folded = sem("folded")
        w1_zero = sem("w1_zero")
        et_zero = sem("et_zero")
        dve_consts = sem("dve_consts")
        idh_ready = sem("idh_ready")
        b2_in = sem("b2_in")
        b2_step = sem("b2_step")
        w1_sum = sem("w1_sum")
        hi_ready = sem("hi_ready")
        lo_ready = [sem(f"lo_ready{i}") for i in range(NO)]
        onehot_ready = sem("onehot_ready")
        staged = sem("staged")
        stage_taken = sem("stage_taken")
        ids_spread = sem("ids_spread")
        ids_placed = sem("ids_placed")
        look_done = sem("look_done")
        look_taken = sem("look_taken")
        gram_done = sem("gram_done")
        gram_act = sem("gram_act")
        gram_dve = sem("gram_dve")
        h1_done = sem("h1_done")
        h1_taken = sem("h1_taken")
        h2_done = sem("h2_done")
        y_ready = sem("y_ready")
        y_out = sem("y_out")

        block = ctx.enter_context(nc.Block())

        def et(t):
            return ET[:, t, :].rearrange("d (b v) -> d b v", v=VP)

        def et_all(f):
            return ET[:, :, :].rearrange("d t (b v) -> d (t b) v", v=VP)[:, :, f]

        STAGED = ["dense"] + [f"T{t}_{g}" for t in range(T) for g in range(len(GROUPS))]

        BESIDE_GRAM = {0: {1: (1,), 2: (2,)}, 1: {0: (0,), 1: (1,), 2: (2,)}, 2: {0: (0,), 2: (1,)}}
        AFTER_DENSE = {0: (3,), 1: (3,)}

        def look_bank(i):
            return hidden[i % 2][:, :]

        IDS_BANK = [gram[0][:, 0, :], gram[0][:, 1, :], gram[1][:, 0, :], gram[1][:, 1, :],
                    second[:, :], stage[:, :], look_bank(1)]
        FIRST_IDS = len(IDS_BANK)
        IDS_BANK += IDS_BANK[:NO - FIRST_IDS]

        def taken(name):
            return stage_taken, STAGED.index(name) + 1

        def load_table(engine, i):
            tab = tables[ONEHOT[i]].rearrange("(p k) d -> p (k d)", k=KR)
            engine.dma_start(raw[0:112, i % RAW, :], tab[0:112, :]).then_inc(table_in[i], 16)
            engine.dma_start(raw[112:PR, i % RAW, :], tab[112:PR, :]).then_inc(table_in[i], 16)

        W1_FIRST = 16 * (3 * FOLDED + 2)
        W1_LOADS = W1_FIRST + 16 * FOLDED

        @block.sync
        def _(sp):
            sp.dma_start(idx[:, :], ids.rearrange("(p t) f -> p (t f)", t=T)).then_inc(ids_in, 16)
            for i in range(RAW):
                load_table(sp, i)
                if i == 1:
                    sp.dma_start(dense_rows[:, :, :], dense.rearrange("(p t) d -> p t d", t=T)).then_inc(dense_in, 16)
                    sp.dma_start(W1d[:, 0, :], w1[0:D, :]).then_inc(w1d_in, 16)
                    sp.dma_start(W1d[:, 1, :], w1[TAIL0:TAIL0 + D, :]).then_inc(w1d_in, 16)
            sp.dma_start(b1c[:, :], b1.rearrange("(c p) -> p c", p=P), allow_slow_non_contiguous=True).then_inc(w1d_in, 16)
            for n in range(3):
                sp.dma_start(b2s[n:n + 1, :], b2.rearrange("(o n) -> o n", o=1)).then_inc(b2_in, 16)
            sp.wait_ge(w1_zero, 1)
            for a in range(FOLDED):
                r0 = pair_row(a) + FOLDED - a - 1
                sp.dma_start(W1s[a:a + 97:32, 0:FOLD, :],
                             w1[r0:r0 + FOLDED, :].rearrange("(m q) n -> q m n", q=4)).then_inc(w1_in, 16)
                sp.dma_start(W1s[a:a + 33:32, FOLD, :], w1[r0 + FOLDED:r0 + FOLDED + 2, :]).then_inc(w1_in, 16)
            for j in range(FOLDED):
                f, q, m = j + FOLDED, j % 4, j // 4
                sp.dma_start(W1s[32 * q + f + 1:32 * q + NF, m, :],
                             w1[pair_row(f):pair_row(f) + NF - 1 - f, :]).then_inc(w1_in, 16)
            sp.dma_start(W1s[32 + NF - 2:32 + NF - 1, FOLD, :], w1[TAIL0 - 1:TAIL0, :]).then_inc(w1_in, 16)
            sp.dma_start(W1s[64:64 + NF, FOLD, :], w1[D:D + NF, :]).then_inc(w1_in, 16)
            sp.wait_ge(w1_in, W1_FIRST)
            for j in range(FOLDED):
                q, m = j % 4, j // 4
                sp.dma_start(W1s[32 * q + j + 1:32 * q + j + FOLDED, m, :],
                             w1[pair_row(j):pair_row(j) + FOLDED - 1, :]).then_inc(w1_in, 16)
            sp.dma_start(W2s[:, :, :], w2.rearrange("(c p) n -> p c n", p=P)).then_inc(w2_in, 16)
            sp.dma_start(W3b[:, :], w3.rearrange("(o n) c -> o (n c)", o=1).broadcast_to([P, H2])).then_inc(w2_in, 16)
            sp.wait_ge(y_ready, T)
            sp.dma_start(out.rearrange("(p t) o -> p (t o)", t=T), y[:, :]).then_inc(y_out, 16)
            sp.wait_ge(y_out, 16)

        W2_LOADS = 16 * 2

        @block.gpsimd
        def _(pool):
            pool.memset(ident[:, :], 0.0).then_inc(ident_zero, 1)
            pool.iota(row_i[:, :], pattern=[[0, 1]], base=0, channel_multiplier=-KR).then_inc(rows_ready, 1)
            pool.iota(behind_i[:, :], pattern=[[-4, FOLD]], base=0, channel_multiplier=1).then_inc(behind_ready, 1)
            pool.wait_ge(ident_zero, 1)
            pool.affine_select(out=ident[:, :], in_=ident[:, :], compare_op=ALU.not_equal, fill=1.0,
                               base=0, pattern=[[-1, P]], channel_multiplier=1).then_inc(ident_ready, 1)
            pool.wait_ge(ids_in, 16)
            for t in range(T):
                for g in range(len(GROUPS)):
                    if t >= 2:
                        pool.wait_ge(*taken(f"T{t - 2}_{g}"))
                    for f in group_of(t, g):
                        pool.indirect_dma_start(
                            out=rows[:, t % 2, GATHERED.index(f), :], out_offset=None, in_=tables[f],
                            in_offset=bass.IndirectOffsetOnAxis(ap=idx[:, t * NF + f:t * NF + f + 1], axis=0),
                        ).then_inc(gathered[t][g], 16)

        @block.tensor
        def _(pe):
            def spread_ids(i):
                if i >= FIRST_IDS:
                    pe.wait_ge(ids_placed, i - FIRST_IDS + 1)
                for t in range(looked_up(i).start // P, T):
                    c = t * NF + ONEHOT[i]
                    last = pe.matmul(IDS_BANK[i][:, P * t:P * (t + 1)], idh[:, c:c + 1].broadcast_to([P, P]), ident_h[:, :],
                                     start=True, stop=True)
                last.then_inc(ids_spread, 1)

            def look_up(i):
                if i >= 2:
                    pe.wait_ge(look_taken, i - 1)
                elif i == 1:
                    pe.wait_ge(ids_placed, FIRST_IDS)
                pe.wait_ge(hi_ready, i + 1)
                pe.wait_ge(lo_ready[i], 1)
                for k in range(KR):
                    pe.wait_ge(onehot_ready, KR * i + k + 1)
                    for n in range(2):
                        last = pe.matmul(look_bank(i)[:, looked_up(i)], part[0:PR, i % 2, n, D * k:D * (k + 1)],
                                         onehot[0:PR, i % 2, k, looked_up(i)],
                                         start=(k == 0 and n == 0), stop=(k == KR - 1 and n == 1))
                last.then_inc(look_done, 1)

            def transposes(t, g):
                pe.wait_ge(stage_taken, STAGED.index(f"T{t}_{g}"))
                pe.wait_ge(gathered[t][g], 16 * len(group_of(t, g)))
                for n, f in enumerate(group_of(t, g)):
                    last = pe.transpose(stage[:, P * n:P * (n + 1)], rows[:, t % 2, GATHERED.index(f), :], ident[:, :])
                last.then_inc(staged, 1)

            def gram_group(n):
                t, j0 = n // GG, n % GG * 2 * GP
                if n >= 2:
                    pe.wait_ge(gram_act, n - 1)
                    pe.wait_ge(gram_dve, n - 1)
                if t and n % GG == 0:
                    pe.wait_ge(h1_taken, HC * (t - 1) + 2)
                for j in range(2 * GP):
                    at = (j % GP) * 4 * NV
                    last = pe.matmul(gram[n % 2][:, j // GP, at:at + 4 * NV],
                                     ET[:, t, 4 * VP * (j0 + j):4 * VP * (j0 + j + 1)],
                                     et(t)[:, 4 * (j0 + j):4 * (j0 + j) + 4, 0:NV],
                                     start=True, stop=True)
                last.then_inc(gram_done, 1)

            def dense_part(t):
                if t:
                    pe.wait_ge(h1_taken, HC * t)
                else:
                    pe.wait_ge(look_taken, NO)
                    pe.wait_ge(w1_sum, 1)
                pe.wait_ge(gram_act, GG * (t + 1) - 1)
                pe.wait_ge(gram_dve, GG * (t + 1) - 1)
                for c in range(HC):
                    pe.matmul(H1_BANKS[c][:, 0:P], W1e[:, P * c:P * (c + 1)], et(t)[:, :, DENSE], start=True, stop=False)

            def layer1(t, c):
                if t == 0 and c == 0:
                    pe.wait_ge(w1_in, W1_LOADS)
                if c == 0:
                    pe.wait_ge(folded, GG * (t + 1))
                for s in range(WSLOTS):
                    k, z_slot = (P, s) if s < FOLD else (32 * (NV - 4 * (SLOTS - 1)), SLOTS - 1)
                    last = pe.matmul(H1_BANKS[c][:, 0:P], W1s[0:k, s, P * c:P * (c + 1)], Z[0:k, t % 2, z_slot, :],
                                     start=False, stop=(s == WSLOTS - 1))
                last.then_inc(h1_done, 1)

            def layer2(t, c):
                if c == 0:
                    if t == 0:
                        pe.wait_ge(w2_in, W2_LOADS)
                        pe.wait_ge(b2_step, 7)
                        pe.wait_ge(ids_placed, NO)
                    else:
                        pe.wait_ge(y_ready, t)
                    pe.matmul(second[:, 0:H2], ones[:, :], b2k[:, :], start=True, stop=False)
                pe.wait_ge(h1_taken, HC * t + c + 1)
                last = pe.matmul(second[:, 0:H2], h1T[:, t % 2, c, :], W2s[:, c, :], start=False, stop=(c == HC - 1))
                if c == HC - 1:
                    last.then_inc(h2_done, 1)

            pe.wait_ge(idh_ready, 2)
            for i in range(FIRST_IDS):
                spread_ids(i)
            for i in range(NO):
                look_up(i)
                if 1 <= i <= len(GROUPS):
                    transposes(0, i - 1)
                if i == 0:
                    pe.wait_ge(ident_ready, 1)
                    pe.wait_ge(dense_in, 16)
                    pe.wait_ge(ids_placed, FIRST_IDS)
                    for t in range(T):
                        last = pe.transpose(stage[:, P * t:P * (t + 1)], dense_rows[:, t, :], ident[:, :])
                    last.then_inc(staged, 1)
                    for later in range(FIRST_IDS, NO):
                        spread_ids(later)
            transposes(1, 0)
            for t in range(T):
                more = t + 1 < T
                if t == 0:
                    pe.wait_ge(look_taken, NO)
                    pe.wait_ge(et_zero, T)
                pe.wait_ge(*taken(f"T{t}_{len(GROUPS) - 1}"))
                for n in range(GG):
                    gram_group(GG * t + n)
                    for g in BESIDE_GRAM.get(t, {}).get(n, ()):
                        transposes(t + 1, g)
                dense_part(t)
                if t:
                    layer2(t - 1, 3)
                for g in AFTER_DENSE.get(t, ()):
                    transposes(t + 1, g)
                layer1(t, 0)
                if t == T - 2:
                    transposes(t + 1, 2)
                layer1(t, 1)
                layer2(t, 0)
                if more:
                    transposes(t + 1, 3 if t == T - 2 else 4)
                layer1(t, 2)
                layer2(t, 1)
                if more:
                    transposes(t + 1, 4 if t == T - 2 else 5)
                layer1(t, 3)
                layer2(t, 2)
                if t == T - 2:
                    transposes(t + 1, 5)
            layer2(T - 1, 3)

        def columns_of(bank, t, g):
            group = group_of(t, g)
            n = len(group)
            return (bank[:, 0:P * n].rearrange("d (f b) -> d b f", f=n),
                    et(t)[:, :, group[0]:group[0] + n])

        def z_moves(n, samples):
            t, j0 = n // GG, n % GG * 2 * GP
            for q in range(4):
                ns = len(range(q, NV, 4))
                for i in samples:
                    src = gram[n % 2][32 * i:32 * i + 32, :, 0:GP * 4 * NV].rearrange(
                        "p b (j i c) -> p b j i c", i=4, c=NV)[:, :, :, i, q:q + 4 * (ns - 1) + 1:4]
                    dst = Z[32 * q:32 * q + 32, t % 2, 0:ns, 4 * j0:4 * (j0 + 2 * GP)].rearrange(
                        "p s (b j i) -> p b j s i", b=2, i=4)[:, :, :, :, i]
                    yield dst, src

        @block.scalar
        def _(act):
            def take(name):
                act.wait_ge(staged, STAGED.index(name) + 1)

            def take_look_up(i):
                act.wait_ge(look_done, i + 1)
                act.copy(et_all(ONEHOT[i])[:, looked_up(i)], look_bank(i)[:, looked_up(i)]).then_inc(look_taken, 1)

            def take_transposes(t, g):
                take(f"T{t}_{g}")
                src, dst = columns_of(stage, t, g)
                act.copy(dst, src).then_inc(stage_taken, 1)

            def place_in_chunk(i):
                if i == 0:
                    act.wait_ge(rows_ready, 2)
                act.wait_ge(ids_spread, i + 1)
                act.activation(idb[:, i, looked_up(i)], IDS_BANK[i][:, looked_up(i)], ACT.Identity, bias=first_row[:, :]).then_inc(ids_placed, 1)

            def upper_part(i):
                act.wait_ge(table_in[i], 32)
                if i >= 2:
                    act.wait_ge(look_done, i - 1)
                act.copy(part[0:PR, i % 2, 0, :], raw[0:PR, i % RAW, :]).then_inc(hi_ready, 1)

            def move_gram(n):
                act.wait_ge(gram_done, n + 1)
                if n >= 2 * GG:
                    act.wait_ge(h1_done, HC * (n // GG - 1))
                for dst, src in z_moves(n, (2, 3)):
                    last = act.copy(dst, src)
                last.then_inc(gram_act, 1)

            act.wait_ge(dve_consts, 1)
            act.activation(warm[:, :], zero[:, :], ACT.Identity, bias=zero[:, :])
            place_in_chunk(0)
            upper_part(0)
            upper_part(1)
            for i in range(1, FIRST_IDS):
                place_in_chunk(i)
            for i in range(NO):
                if i + RAW < NO:
                    act.wait_ge(lo_ready[i], 1)
                    load_table(act, i + RAW)
                take_look_up(i)
                if i == 0:
                    take("dense")
                    act.copy(et_all(DENSE), stage[:, :]).then_inc(stage_taken, 1)
                if i + 2 < NO:
                    upper_part(i + 2)
                if 1 <= i <= len(GROUPS):
                    take_transposes(0, i - 1)
                if i == 1:
                    for later in range(FIRST_IDS, NO):
                        place_in_chunk(later)
                if 2 <= i < 2 + T:
                    act.copy(et(i - 2)[:, :, NV:VP],
                             zero[:, :].broadcast_to([P, P * (VP - NV)]).rearrange("d (b v) -> d b v", v=VP - NV)).then_inc(et_zero, 1)
            take_transposes(1, 0)
            for t in range(T):
                more = t + 1 < T
                for n in range(GG):
                    move_gram(GG * t + n)
                    for g in BESIDE_GRAM.get(t, {}).get(n, ()):
                        take_transposes(t + 1, g)
                if more:
                    for g in range(2 if t == T - 2 else 3, len(GROUPS)):
                        take_transposes(t + 1, g)

        @block.vector
        def _(dve):
            def take_h1(t, c):
                dve.wait_ge(h1_done, HC * t + c + 1)
                dve.tensor_scalar(h1T[:, t % 2, c, :], H1_BANKS[c][:, 0:P], b1c[:, c:c + 1], 0.0,
                                  ALU.add, ALU.max).then_inc(h1_taken, 1)

            def last_layer(t):
                dve.wait_ge(h2_done, t + 1)
                dve.wait_ge(w2_in, W2_LOADS)
                dve.scalar_tensor_tensor(out=h2w[:, :], in0=second[:, 0:H2], scalar=0.0, in1=W3b[:, :],
                                         op0=ALU.max, op1=ALU.mult, accum_out=y[:, t:t + 1]).then_inc(y_ready, 1)

            def make_onehot(i, chunks):
                dve.wait_ge(ids_placed, i + 1)
                if i >= 2:
                    dve.wait_ge(look_done, i - 1)
                for k in chunks:
                    dve.tensor_scalar(onehot[0:PR, i % 2, k, looked_up(i)], idb[0:PR, i, looked_up(i)], float(k), None,
                                      ALU.is_equal).then_inc(onehot_ready, 1)

            def lower_part(i):
                dve.wait_ge(table_in[i], 32)
                dve.wait_ge(hi_ready, i + 1)
                dve.tensor_tensor(part[0:PR, i % 2, 1, :], raw[0:PR, i % RAW, :], part[0:PR, i % 2, 0, :].bitcast(F32),
                                  ALU.subtract).then_inc(lo_ready[i], 1)

            def move_gram(n):
                dve.wait_ge(gram_done, n + 1)
                if n >= 2 * GG:
                    dve.wait_ge(h1_done, HC * (n // GG - 1))
                for dst, src in z_moves(n, (0, 1)):
                    last = dve.tensor_copy(dst, src)
                last.then_inc(gram_dve, 1)

            def fold(n):
                t, at = n // GG, slice(8 * GP * (n % GG), 8 * GP * (n % GG + 1))
                dve.wait_ge(gram_act, n + 1)
                dve.wait_ge(gram_dve, n + 1)
                dve.copy_predicated(Z[:, t % 2, 0:FOLD, at], fold_mask[:, :, :], Z[:, t % 2, FOLD:2 * FOLD, at]).then_inc(folded, 1)

            dve.memset(zero[:, :], 0.0).then_inc(dve_consts, 1)
            dve.memset(W1s[:, :, :], 0.0).then_inc(w1_zero, 1)
            dve.wait_ge(ident_ready, 1)
            dve.tensor_copy(ident_h[:, :], ident[:, :]).then_inc(idh_ready, 1)
            dve.wait_ge(ids_in, 16)
            dve.tensor_copy(idh[:, :], idx[:, :]).then_inc(idh_ready, 1)
            dve.wait_ge(rows_ready, 1)
            dve.tensor_copy(first_row[:, :], row_i[:, :]).then_inc(rows_ready, 1)
            for i in range(NO):
                early = 0
                if i == 0:
                    early = 2
                    make_onehot(i, range(early))
                lower_part(i)
                make_onehot(i, range(early, KR))
            dve.wait_ge(w1d_in, 48)
            dve.tensor_tensor(W1e[:, :], W1d[:, 0, :], W1d[:, 1, :], ALU.add).then_inc(w1_sum, 1)
            dve.memset(ones[:, :], 1.0).then_inc(dve_consts, 1)
            dve.wait_ge(b2_in, 48)
            dve.tensor_copy(b2p[:, 0, :], b2s[:, :]).then_inc(b2_step, 1)
            dve.wait_ge(b2_step, 1)
            dve.tensor_tensor(b2m[:, 0, :], b2s[:, :], b2p[:, 0, :], ALU.subtract).then_inc(b2_step, 1)
            dve.wait_ge(b2_step, 2)
            dve.tensor_copy(b2p[:, 1, :], b2m[:, 0, :]).then_inc(b2_step, 1)
            dve.wait_ge(b2_step, 3)
            dve.tensor_tensor(b2m[:, 1, :], b2m[:, 0, :], b2p[:, 1, :], ALU.subtract).then_inc(b2_step, 1)
            dve.wait_ge(b2_step, 4)
            dve.tensor_copy(b2k[0:3, :], b2m[:, 1, :]).then_inc(b2_step, 1)
            dve.wait_ge(b2_step, 5)
            dve.tensor_copy(b2k[0:2, :], b2p[0:2, 1, :]).then_inc(b2_step, 1)
            dve.wait_ge(b2_step, 6)
            dve.tensor_copy(b2k[0:1, :], b2p[0:1, 0, :]).then_inc(b2_step, 1)
            dve.wait_ge(behind_ready, 1)
            for q in range(4):
                last = dve.tensor_scalar(behind[32 * q:32 * q + 32, :], behind_i[32 * q:32 * q + 32, :], 33.0 * q, None, ALU.subtract)
            last.then_inc(mask_step, 1)
            dve.wait_ge(mask_step, 1)
            dve.scalar_tensor_tensor(out=fold_f[:, :], in0=behind[:, :], scalar=float(FOLDED + 1), in1=behind[:, :],
                                     op0=ALU.subtract, op1=ALU.mult).then_inc(mask_step, 1)
            dve.wait_ge(mask_step, 2)
            for m in range(FOLD):
                last = dve.tensor_scalar(fold_mask[:, m, :], fold_f[:, m:m + 1].broadcast_to([P, 8 * GP]), 0.0, None, ALU.is_ge)
            last.then_inc(mask_step, 1)
            for t in range(T):
                more = t + 1 < T
                for n in range(GG):
                    move_gram(GG * t + n)
                    fold(GG * t + n)
                if t:
                    last_layer(t - 1)
                for c in range(HC):
                    take_h1(t, c)
            last_layer(T - 1)


_INPUTS = (['r_dense_features', 'ids'] + [f'tbl_{f}' for f in range(NF)]
           + ['W_top1', 'b_top1', 'W_top2', 'b_top2', 'W_top3'])


def kernel(**inputs):
    import numpy as np
    import concourse.bacc as bacc
    from concourse.bass_utils import run_bass_kernel_spmd

    nc = bacc.Bacc("TRN2", target_bir_lowering=False, num_devices=1)
    arrays, aps = {}, []
    for name in _INPUTS:
        a = np.ascontiguousarray(inputs[name])
        arrays[name] = a
        aps.append(nc.dram_tensor(name, a.shape, mybir.dt.from_np(a.dtype), kind="ExternalInput").ap())
    out = nc.dram_tensor("out", (B, 1), F32, kind="ExternalOutput").ap()
    dlrm_tower(nc, aps[0], aps[1], aps[2:2 + NF], *aps[2 + NF:], out)
    r = run_bass_kernel_spmd(nc, [arrays], core_ids=[0])
    return r.results[0]["out"]
```
